# Optimizing a Trainium2 kernel written in Bass

```python
import numpy as np
import jax
import jax.numpy as jnp

def _softmax(x, axis=-1):
    return jax.nn.softmax(x, axis=axis)

def _gelu(x):
    return jax.nn.gelu(x, approximate=True)

def _silu(x):
    return jax.nn.silu(x)

def _sigmoid(x):
    return jax.nn.sigmoid(x)

def _layernorm(x, axis=-1, eps=1e-05):
    m = jnp.mean(x, axis=axis, keepdims=True)
    v = jnp.var(x, axis=axis, keepdims=True)
    return (x - m) / jnp.sqrt(v + eps)

def _scatter_add(tgt, idx, src, axis=0):
    return tgt.at[idx].add(src)

def _segment_sum(src, seg, n):
    return jax.ops.segment_sum(src, seg, n)
kernel_name = 'mk_gnn_resnorm_d2_gnn_r8_4a3870'

def setup_inputs(seed: int=0):
    np.random.seed(seed)
    _w = jnp.asarray

    def _rec_inputs():
        import jax
        import jax.numpy as jnp
        _gk = jax.random.key(seed)
        x = -0.000202 + 1 * jax.random.normal(jax.random.fold_in(_gk, 1), (12500, 64), jnp.float32)
        src = jax.random.randint(jax.random.fold_in(_gk, 2), (200000,), 0, 12500, jnp.int32)
        dst = jnp.minimum((12500 * jax.random.uniform(jax.random.fold_in(_gk, 3), (200000,)) ** 2.0).astype(jnp.int32), 99999)
        _o = jnp.argsort(dst, stable=True)
        src = src[_o]
        dst = dst[_o]
        edge_attr_32 = 0.000102155 + 1.00015 * jax.random.normal(jax.random.fold_in(_gk, 13), (200000, 32), jnp.float32)
        edge_type_8 = jax.random.randint(jax.random.fold_in(_gk, 15), (200000,), 0, 8, jnp.int32)
        return (x, src, dst, edge_attr_32, edge_type_8)
    x, src, dst, edge_attr_32, edge_type_8 = _rec_inputs()

    def _L0_gnn_setup():
        import jax, jax.numpy as jnp
        import numpy as np
        N_NODES = 12500
        N_EDGES = 125000
        N_GRAPHS = 16
        D_NODE = 64
        D_EDGE = 32
        D_GLOB = 32
        OUT_DIM = 64
        IN1 = 2 * D_NODE + D_EDGE + D_GLOB
        IN2 = D_NODE + OUT_DIM + D_GLOB
        key = jax.random.key(seed)
        ks = jax.random.split(key, 9)
        x = jax.random.normal(ks[0], (N_NODES, D_NODE), dtype=jnp.float32)
        edge_index = jax.random.randint(ks[1], (2, N_EDGES), 0, N_NODES, dtype=jnp.int64 if jax.config.jax_enable_x64 else jnp.int32)
        edge_attr = jax.random.normal(ks[2], (N_EDGES, D_EDGE), dtype=jnp.float32)
        u = jax.random.normal(ks[3], (N_GRAPHS, D_GLOB), dtype=jnp.float32)
        batch = jnp.sort(jax.random.randint(ks[4], (N_NODES,), 0, N_GRAPHS))
        W1 = jax.random.normal(ks[5], (IN1, OUT_DIM), dtype=jnp.float32) / np.sqrt(IN1)
        b1 = jnp.zeros((OUT_DIM,), dtype=jnp.float32)
        W2 = jax.random.normal(ks[6], (IN2, OUT_DIM), dtype=jnp.float32) / np.sqrt(IN2)
        b2 = jnp.zeros((OUT_DIM,), dtype=jnp.float32)
        return {'x': x, 'edge_index': edge_index, 'edge_attr': edge_attr, 'u': u, 'batch': batch, 'W1': W1, 'b1': b1, 'W2': W2, 'b2': b2}
    _L0_gnn_all = _L0_gnn_setup()
    _L0_gnn_in = {k: v for k, v in _L0_gnn_all.items() if k in ('u', 'W1', 'b1', 'W2', 'b2')}
    del _L0_gnn_all

    def _L1_gnn_setup():
        import jax, jax.numpy as jnp
        import numpy as np
        N_NODES = 6250
        N_EDGES = 100000
        IN_DIM = 64
        OUT_DIM = 64
        NUM_RELS = 8
        key = jax.random.key(seed)
        k1, k2, k3, k4, k5, k6 = jax.random.split(key, 6)
        h = jax.random.normal(k1, (N_NODES, IN_DIM), dtype=jnp.float32)
        fc_weight = jax.random.normal(k2, (NUM_RELS, IN_DIM, OUT_DIM), dtype=jnp.float32) * 0.1
        attn_weight = jax.random.normal(k3, (NUM_RELS, 2 * OUT_DIM, 1), dtype=jnp.float32) * 0.1
        src = jax.random.randint(k4, (N_EDGES,), 0, N_NODES, dtype=jnp.int32)
        dst = jax.random.randint(k5, (N_EDGES,), 0, N_NODES, dtype=jnp.int32)
        etype = jax.random.randint(k6, (N_EDGES,), 0, NUM_RELS, dtype=jnp.int32)
        return {'h': h, 'fc_weight': fc_weight, 'attn_weight': attn_weight, 'src': src, 'dst': dst, 'etype': etype}
    _L1_gnn_all = _L1_gnn_setup()
    _L1_gnn_in = {k: v for k, v in _L1_gnn_all.items() if k in ('fc_weight', 'attn_weight')}
    del _L1_gnn_all
    return {'x': x, 'src': src, 'dst': dst, 'edge_attr_32': edge_attr_32, 'edge_type_8': edge_type_8, 'L0_gnn_u': _L0_gnn_in['u'], 'L0_gnn_W1': _L0_gnn_in['W1'], 'L0_gnn_b1': _L0_gnn_in['b1'], 'L0_gnn_W2': _L0_gnn_in['W2'], 'L0_gnn_b2': _L0_gnn_in['b2'], 'L1_gnn_fc_weight': _L1_gnn_in['fc_weight'], 'L1_gnn_attn_weight': _L1_gnn_in['attn_weight']}

def reference(x, src, dst, edge_attr_32, edge_type_8, L0_gnn_u, L0_gnn_W1, L0_gnn_b1, L0_gnn_W2, L0_gnn_b2, L1_gnn_fc_weight, L1_gnn_attn_weight):
    import jax
    import jax.numpy as jnp

    def _L0_gnn_ref(x, edge_index, edge_attr, u, batch, W1, b1, W2, b2):
        import jax, jax.numpy as jnp
        import numpy as np
        N_NODES = 12500
        N_EDGES = 125000
        N_GRAPHS = 16
        D_NODE = 64
        D_EDGE = 32
        D_GLOB = 32
        OUT_DIM = 64
        IN1 = 2 * D_NODE + D_EDGE + D_GLOB
        IN2 = D_NODE + OUT_DIM + D_GLOB
        src = edge_index[0]
        dst = edge_index[1]
        u_per_node = u[batch]
        all_feat = jnp.concatenate([x[dst], x[src], edge_attr, u_per_node[dst]], axis=-1)
        msg = jax.nn.relu(all_feat @ W1 + b1)
        agg = jax.ops.segment_sum(msg, dst, num_segments=x.shape[0])
        node_in = jnp.concatenate([x, agg, u_per_node], axis=-1)
        return jax.nn.relu(node_in @ W2 + b2)

    def _L1_gnn_ref(h, fc_weight, attn_weight, src, dst, etype):
        import jax, jax.numpy as jnp
        import numpy as np
        N_NODES = 6250
        N_EDGES = 100000
        IN_DIM = 64
        OUT_DIM = 64
        NUM_RELS = 8
        N = h.shape[0]
        Z = jnp.einsum('ni,rio->nro', h, fc_weight)
        z_s = Z[src, etype]
        z_d = Z[dst, etype]
        aw = attn_weight[etype, :, 0]
        z2 = jnp.concatenate([z_s, z_d], axis=1)
        e = jax.nn.relu(jnp.sum(z2 * aw, axis=1))
        m = jax.ops.segment_max(e, dst, num_segments=N)
        ex = jnp.exp(e - m[dst])
        denom = jax.ops.segment_sum(ex, dst, num_segments=N)
        alpha = ex / denom[dst]
        h_out = jax.ops.segment_sum(alpha[:, None] * z_s, dst, num_segments=N)
        return h_out
    edge_index = jnp.stack([src, dst])
    batch0 = jnp.zeros((12500,), jnp.int32)
    x = _layernorm(x + _L0_gnn_ref(x, edge_index, edge_attr_32, L0_gnn_u, batch0, L0_gnn_W1, L0_gnn_b1, L0_gnn_W2, L0_gnn_b2), axis=-1)
    x = _layernorm(x + _L1_gnn_ref(x, L1_gnn_fc_weight, L1_gnn_attn_weight, src, dst, edge_type_8), axis=-1)
    return x

_drawn_inputs = setup_inputs


def setup_inputs(seed=0):
    import zlib

    import numpy as np

    out = dict(_drawn_inputs(seed))
    spreads = {'L0_gnn_b1': (0.0, 0.1), 'L0_gnn_b2': (0.0, 0.276)}
    factors = {}
    for name, (base, spread) in spreads.items():
        noise = np.random.default_rng([zlib.crc32(name.encode()), seed]).standard_normal(out[name].shape)
        drawn = base * np.exp(spread * noise) if base else spread * noise
        out[name] = jnp.asarray(drawn.astype(out[name].dtype))
    for name, factor in factors.items():
        out[name] = (out[name] * factor).astype(out[name].dtype)
    return out
```

```python
import concourse.bass as bass
from concourse import mybir
from contextlib import ExitStack

F32 = mybir.dt.float32
BF16 = mybir.dt.bfloat16
I32 = mybir.dt.int32
ALU = mybir.AluOpType
ACT = mybir.ActivationFunctionType
AXX = mybir.AxisListType.X

P = 128
N = 12500
D = 64
DE = 32
R = 8
E = 200000
NB = -(-N // P)
NP = NB * P
NT = -(-E // P)
O = 8
TO = -(-NT // O)
EP = TO * O * P
NTP = TO * O
SO = -(-(NT + NB - 1) // (4 * O)) * 4
NS = SO * O
SC = NS // P
RING = 160
ZW = D + 2
DST_PAD = 16000
EPS = 1e-5
Q = 4
LEAD = RING // O - (2 * O - 2 + NB - 1) // O
assert NS >= NT + NB - 1 and NS % P == 0 and TO % Q == 0 and SO % Q == 0


def take(e, sem, n=1):
    e.wait_ge(sem, n).then_inc(sem, -n)


class Chain:

    def __init__(self, e, sem):
        self.e, self.sem = e, sem

    def __call__(self, ins):
        ins.then_inc(self.sem, 1)
        take(self.e, self.sem)


def bank(ctx, nc, name, shape):
    t = ctx.enter_context(nc.psum_tensor(name, [P, 512], F32))
    n = 1
    for w in shape[1:]:
        n *= w
    v = t[0:shape[0], 0:n]
    return v.rearrange("p (a b) -> p a b", b=shape[2]) if len(shape) == 3 else v


def phase_inputs(nc, A):
    with ExitStack() as ctx:
        sem = lambda n: ctx.enter_context(nc.semaphore(n))
        sb = lambda n, s, d: ctx.enter_context(nc.sbuf_tensor(n, s, d))
        cur = sb("chk_cur", [P, NTP], I32)
        nxt = sb("chk_nxt", [P, NTP], I32)
        gt = sb("chk_gt", [P, NTP], F32)
        cnt = sb("chk_cnt", [P, 1], F32)
        awb = sb("aw_bcast", [D, R, 2 * D], F32)
        fct = sb("fc_rel", [D, R, D], F32)
        prod = sb("fc_aw", [D, R, D], F32)
        u0c = sb("u0_cols", [DE, D + 1], F32)
        wu = sb("w_u", [DE, 2 * D], F32)
        bb = sb("b_rows", [D + 1, 2 * D], F32)
        pcnt = bank(ctx, nc, "p_cnt", [1, 1])
        pu = bank(ctx, nc, "p_u", [D + 1, 2 * D])
        pu0 = bank(ctx, nc, "p_u0", [1, 2 * D])
        s_chk, s_w, s_z, s_id, s_v, s_pe, s_pc, s_b0 = (sem(n) for n in (
            "in_chk", "in_w", "in_zeroed", "in_ident", "in_dve", "in_pe", "in_cnt", "in_b2"))
        block = ctx.enter_context(nc.Block())

        @block.sync
        def _(e):
            e.dma_start(cur[:, :], A.dst_in[0:EP].rearrange("(p c) -> p c", p=P)).then_inc(s_chk, 16)
            e.dma_start(nxt[:, :], A.dst_in[1:EP + 1].rearrange("(p c) -> p c", p=P)).then_inc(s_chk, 16)
            e.dma_start(A.XA[:, 0:NB, 0:D], A.x_in.rearrange("(b p) d -> p b d", p=P)).then_inc(s_w, 16)
            e.dma_start(fct[:, :, :], A.fc_in.rearrange("r i o -> i r o")).then_inc(s_w, 16)
            e.dma_start(awb[:, :, :], A.aw_in.rearrange("r c z -> (r c z)").partition_broadcast(D)
                        .rearrange("p (r c) -> p r c", r=R)).then_inc(s_w, 16)
            e.dma_start(A.W2ab[:, :], A.W2_in[0:2 * D, :]).then_inc(s_w, 16)
            e.dma_start(A.rhs0[0:D, 0:D], A.W1_in[0:D, :]).then_inc(s_w, 16)
            e.dma_start(A.rhs0[0:D, D:2 * D], A.W1_in[D:2 * D, :]).then_inc(s_w, 16)
            e.dma_start(wu[:, 0:D], A.W1_in[2 * D + DE:2 * D + 2 * DE, :]).then_inc(s_w, 16)
            e.dma_start(wu[:, D:2 * D], A.W2_in[2 * D:2 * D + DE, :]).then_inc(s_w, 16)
            e.wait_ge(s_z, 1)
            for g in range(4):
                e.dma_start(A.W1c4[DE * g:DE * (g + 1), D * g:D * (g + 1)], A.W1_in[2 * D:2 * D + DE, :]).then_inc(s_w, 16)
            e.dma_start(u0c[:, D:D + 1], A.u_in[0:1, :].rearrange("a f -> f a"), allow_slow_non_contiguous=True).then_inc(s_w, 16)
            e.dma_start(bb[D:D + 1, 0:D], A.b1_in.rearrange("(a d) -> a d", a=1)).then_inc(s_w, 16)
            e.dma_start(A.b2row[0:1, :], A.b2_in.rearrange("(a d) -> a d", a=1)).then_inc(s_b0, 16)
            e.wait_ge(s_w, 16 * 14)
            e.wait_ge(s_b0, 16)

        @block.gpsimd
        def _(e):
            e.memset(u0c[:, :], 0.0)
            e.memset(bb[:, :], 0.0)
            e.memset(A.W1c4[:, :], 0.0)
            e.memset(A.ones[:, :], 1.0)
            e.memset(A.epsb[:, :], EPS)
            e.memset(A.ident[:, :], 0.0).then_inc(s_z, 1)
            e.wait_ge(s_z, 1)
            e.affine_select(out=A.ident[:, :], in_=A.ident[:, :], compare_op=ALU.not_equal, fill=1.0,
                            base=0, pattern=[[-1, P]], channel_multiplier=1)
            e.iota(A.iota[:, :], pattern=[[1, P]], base=0, channel_multiplier=0,
                   allow_small_or_imprecise_dtypes=True)
            e.iota(A.kcol[:, :], pattern=[[P, SC]], base=0, channel_multiplier=1,
                   allow_small_or_imprecise_dtypes=True)
            e.memset(A.XA[:, :, D:2 * D], 0.0)
            e.memset(A.XA[:, NB:NB + 1, 0:D], 0.0).then_inc(s_id, 1)

        @block.vector
        def _(e):
            done = Chain(e, s_v)
            e.wait_ge(s_chk, 32)
            done(e.tensor_tensor(out=gt[:, :], in0=cur[:, :], in1=nxt[:, :], op=ALU.is_gt))
            done(e.tensor_reduce(out=cnt[:, :], in_=gt[:, :], axis=AXX, op=ALU.add))
            e.wait_ge(s_id, 1)
            e.sem_inc(s_pe, 1)
            done(e.memset(A.rhs1[:, :], 0.0))
            z8 = A.rhs1[:, 0:R * ZW].rearrange("i (r c) -> i r c", c=ZW)
            done(e.memset(z8[D:D + 1, :, D:D + 1], 1.0))
            e.wait_ge(s_w, 16 * 14)
            done(e.tensor_copy(z8[0:D, :, 0:D], fct[:, :, :]))
            for half in range(2):
                done(e.tensor_tensor(out=prod[:, :, :], in0=fct[:, :, :],
                                     in1=awb[:, :, half * D:(half + 1) * D], op=ALU.mult))
                out = z8[0:D, :, D + 1:D + 2] if half == 0 else A.rhs1[0:D, R * ZW:R * ZW + R]
                done(e.tensor_reduce(out=out, in_=prod[:, :, :], axis=AXX, op=ALU.add))
            e.wait_ge(s_pc, 1)
            done(e.tensor_copy(A.flag[0:1, 0:1], pcnt[0:1, 0:1]))
            e.wait_ge(s_b0, 16)
            done(e.tensor_tensor(out=A.rhs0[D:D + 1, 0:2 * D], in0=pu[D:D + 1, :], in1=bb[D:D + 1, :], op=ALU.add))
            done(e.memset(A.rhs0[D:D + 1, D:2 * D], 0.0))
            done(e.tensor_tensor(out=A.b2row[0:1, :], in0=pu0[0:1, D:2 * D], in1=A.b2row[0:1, :], op=ALU.add))

        @block.tensor
        def _(e):
            e.wait_ge(s_w, 16 * 14)
            e.wait_ge(s_pe, 1)
            e.matmul(pu[:, :], u0c[:, :], wu[:, :], start=True, stop=True)
            e.matmul(pu0[:, :], u0c[:, D:D + 1], wu[:, :], start=True, stop=True)
            e.matmul(pcnt[:, :], cnt[:, :], A.ones[:, 0:1], start=True, stop=True).then_inc(s_pc, 1)


def descends(e, A, name):
    r = e.alloc_register(name)
    e.reg_load(r, A.flag[0:1, 0:1])
    return e.snap(r, min_val=0, max_val=EP)


def phase_order(nc, A):
    with ExitStack() as ctx:
        sem = lambda n: ctx.enter_context(nc.semaphore(n))
        sb = lambda n, s, d: ctx.enter_context(nc.sbuf_tensor(n, s, d))
        cols = [sb(f"or_{n}", [P, NTP], I32) for n in ("dst", "src", "typ")]
        bi = sb("or_blk_i", [P, NTP], I32)
        bf = sb("or_blk", [P, NTP], F32)
        lower = sb("or_lower", [P, P], F32)
        oh = sb("or_oh", [P, P], F32)
        run = sb("or_run", [P, P], F32)
        at = sb("or_at", [P, P], F32)
        one = sb("or_one", [P, P], F32)
        pos = sb("or_pos", [P, 1], F32)
        posi = sb("or_posi", [P, 1], I32)
        ea = sb("or_ea", [P, DE], F32)
        pc = bank(ctx, nc, "or_pc", [P, P])
        pr = bank(ctx, nc, "or_pr", [P, P])
        s_cp, s_ld, s_v, s_lo, s_oh, s_cnt, s_ea, s_ef, s_pos = (sem("or_" + n) for n in (
            "copied loaded dve lower oh cnt ea ea_free pos").split())
        s_sc = [sem(f"or_scattered{k}") for k in range(4)]
        block = ctx.enter_context(nc.Block())
        flat = lambda a: a.rearrange("t (c z) -> (t c) z", z=1)

        @block.sync
        def _(e):
            bad = descends(e, A, "or_sp")
            with e.If(bad == 0):
                for to, of in ((A.dst_s, A.dst_in), (A.src_s, A.src_in), (A.typ_s, A.typ_in)):
                    e.dma_start(to.rearrange("(p t) c -> p (t c)", p=112), of[0:EP].rearrange("(p c) -> p c", p=112)).then_inc(s_cp, 16)
                e.wait_ge(s_cp, 48)
            with e.Else():
                for to, of in zip(cols, (A.dst_in, A.src_in, A.typ_in)):
                    e.dma_start(to[:, :], of[0:EP].rearrange("(p c) -> p c", p=P)).then_inc(s_ld, 16)
                eav = A.ea_in.rearrange("(p t) f -> p t f", p=P)
                with e.Fori(0, NTP) as t:
                    e.dma_start(ea[:, :], eav[:, bass.ds(t, 1), :]).then_inc(s_ea, 16)
                    for k in range(4):
                        e.wait_ge(s_sc[k], 16 * t + 16)
                    e.sem_inc(s_ef, 1)

        @block.gpsimd
        def _(e):
            bad = descends(e, A, "or_pool")
            with e.If(bad > 0):
                e.memset(lower[:, :], 1.0).then_inc(s_lo, 1)
                e.wait_ge(s_lo, 1)
                e.affine_select(out=lower[:, :], in_=lower[:, :], compare_op=ALU.is_gt, fill=0.0,
                                base=0, pattern=[[1, P]], channel_multiplier=-1).then_inc(s_lo, 1)
                with e.Fori(0, NTP) as t:
                    take(e, s_pos)
                    for k, (col, to) in enumerate(((cols[0], A.dst_s), (cols[1], A.src_s), (cols[2], A.typ_s), (ea, A.ea_s))):
                        src = ea[:, :] if k == 3 else A.or_col[:, k:k + 1]
                        e.indirect_dma_start(out=to if k == 3 else flat(to), in_=src, in_offset=None,
                                             out_offset=bass.IndirectOffsetOnAxis(ap=posi[:, 0:1], axis=0)).then_inc(s_sc[k], 16)

        @block.vector
        def _(e):
            done = Chain(e, s_v)
            bad = descends(e, A, "or_dve")
            with e.If(bad > 0):
                e.wait_ge(s_ld, 48)
                done(e.tensor_scalar(out=bi[:, :], in0=cols[0][:, :], scalar1=7, scalar2=None, op0=ALU.arith_shift_right))
                done(e.tensor_copy(bf[:, :], bi[:, :]))
                done(e.memset(run[:, :], 0.0))
                done(e.memset(one[:, :], 1.0))

                def onehot(t):
                    e.tensor_scalar(out=oh[:, :], in0=A.iota[:, :], scalar1=bf[:, bass.ds(t, 1)], scalar2=None,
                                    op0=ALU.is_equal).then_inc(s_oh, 1)
                with e.Fori(0, NTP) as t:
                    onehot(t)
                    take(e, s_cnt)
                    done(e.tensor_tensor(out=run[:, :], in0=run[:, :], in1=pr[:, :], op=ALU.add))
                done(e.tensor_tensor_scan(out=at[:, :], data0=one[:, :], data1=run[:, :], initial=0.0, op0=ALU.mult, op1=ALU.add))
                done(e.tensor_tensor(out=run[:, :], in0=at[:, :], in1=run[:, :], op=ALU.subtract))
                with e.Fori(0, NTP) as t:
                    onehot(t)
                    take(e, s_cnt)
                    done(e.tensor_tensor(out=at[:, :], in0=run[:, :], in1=pc[:, :], op=ALU.add))
                    done(e.tensor_tensor(out=at[:, :], in0=at[:, :], in1=oh[:, :], op=ALU.mult))
                    done(e.tensor_reduce(out=pos[:, :], in_=at[:, :], axis=AXX, op=ALU.add))
                    done(e.tensor_tensor(out=run[:, :], in0=run[:, :], in1=pr[:, :], op=ALU.add))
                    done(e.tensor_copy(posi[:, :], pos[:, :]))
                    for k in range(3):
                        done(e.tensor_copy(A.or_col[:, k:k + 1], cols[k][:, bass.ds(t, 1)]))
                    e.wait_ge(s_ea, 16 * t + 16)
                    e.sem_inc(s_pos, 1)
                    take(e, s_ef)

        @block.tensor
        def _(e):
            bad = descends(e, A, "or_pe")
            with e.If(bad > 0):
                e.wait_ge(s_lo, 2)
                with e.Fori(0, 2 * NTP) as t:
                    take(e, s_oh)
                    e.matmul(pc[:, :], lower[:, :], oh[:, :], start=True, stop=True)
                    e.matmul(pr[:, :], A.ones[:, :], oh[:, :], start=True, stop=True).then_inc(s_cnt, 1)


def phase_slots(nc, A):
    CH = [(i, min(512, NT - i)) for i in range(0, NT, 512)]
    FULL = NTP // P
    REST = NTP - FULL * P
    with ExitStack() as ctx:
        sem = lambda n: ctx.enter_context(nc.semaphore(n))
        sb = lambda n, s, d: ctx.enter_context(nc.sbuf_tensor(n, s, d))
        fi = sb("first_i", [1, NT], I32)
        li = sb("last_i", [1, NT], I32)
        brf = sb("first_b", [1, NS + 1], F32)
        brd = sb("last_b", [1, NS], F32)
        bf, bl = brf[:, 0:NT], brd[:, 0:NT]
        nn = sb("n_slots", [1, NT], F32)
        on = sb("ones_row", [1, NT], F32)
        ni = sb("n_incl", [1, NT], F32)
        N0, V, dV = on, nn, ni
        Nb = sb("n_bcast", [P, NT], F32)
        dVb = sb("dv_bcast", [P, NT], F32)
        tk = sb("tk", [P, SC], F32)
        vb = sb("vb", [P, SC], F32)
        bk = sb("bk", [P, SC], F32)
        nb128 = sb("nb128", [P, SC], F32)
        tki = sb("tki", [P, SC], I32)
        tr = sb("tr", [P, SC], F32)
        rowi = sb("rowi", [SC, 2, P], I32)
        dg = sb("dst_rows", [P, SC, P], I32)
        tg = sb("typ_rows", [P, SC, P], I32)
        df = sb("dst_f", [P, SC, P], F32)
        tf = sb("typ_f", [P, SC, P], F32)
        junk = df[:, :, :].rearrange("p c k -> p (c k)")[:, 0:NT]
        snat = sb("src_nat", [P, SC, P], I32)
        tnat = sb("typ_nat", [P, SC, P], I32)
        typ = sb("typ_slot", [P, NS], F32)
        ix0 = sb("idx_src", [P, NTP], I32)
        ix1 = sb("idx_z", [P, NTP], I32)
        contb = sb("cont_b", [P, NS], F32)
        ps = [ctx.enter_context(nc.psum_tensor(f"ps_slots{i}", [P, 512], F32)) for i in range(8)]
        s_ld, s_g, s_v, s_p, s_pe, s_dm, s_rw, s_rb, s_done = (sem(n) for n in (
            "sl_load", "sl_gather", "sl_dve", "sl_pool", "sl_pe", "sl_out", "sl_row", "sl_rowback", "sl_dve_to_pe"))
        s_idx = sem("sl_idx")
        s_row2 = sem("sl_row2")
        s_tab = sem("sl_tab")
        block = ctx.enter_context(nc.Block())
        d2 = A.dst_s
        s2 = A.src_s
        t2 = A.typ_s

        @block.sync
        def _(e):
            e.dma_start(fi[0:1, :], d2[0:NT, 0:1].rearrange("t o -> o t"), allow_slow_non_contiguous=True).then_inc(s_ld, 16)
            e.dma_start(li[0:1, :], d2[0:NT, P - 1:P].rearrange("t o -> o t"), allow_slow_non_contiguous=True).then_inc(s_ld, 16)
            for nat, of in ((snat, s2), (tnat, t2)):
                e.dma_start(nat[:, 0:FULL, :], of[0:FULL * P, :].rearrange("(c p) k -> p c k", p=P)).then_inc(s_ld, 16)
                if REST:
                    e.dma_start(nat[0:REST, FULL, :], of[FULL * P:NTP, :]).then_inc(s_ld, 16)
            e.wait_ge(s_rw, 1)
            e.dma_start(A.rows_d[0, :].rearrange("(c p) -> c p", p=P), rowi[:, 0, :]).then_inc(s_rb, 16)
            e.dma_start(A.rows_d[1, :].rearrange("(c p) -> c p", p=P), rowi[:, 1, :]).then_inc(s_rb, 16)
            e.wait_ge(s_rb, 32)
            e.dma_start(A.brow[0:1, :], A.rows_d[0:1, :]).then_inc(s_row2, 16)
            e.dma_start(A.trow[0:1, :], A.rows_d[1:2, :]).then_inc(s_row2, 16)
            e.wait_ge(s_tab, 1)
            e.dma_start(A.typ_d, typ[:, :]).then_inc(s_dm, 16)
            e.dma_start(A.ix1_d, ix1[:, :]).then_inc(s_dm, 16)
            e.dma_start(A.cont_d, contb[:, :]).then_inc(s_dm, 16)
            e.dma_start(A.ix0_d, ix0[:, :]).then_inc(s_dm, 16)
            e.wait_ge(s_dm, 64)
            e.wait_ge(s_row2, 32)

        @block.gpsimd
        def _(e):
            e.wait_ge(s_idx, 1)
            for c in range(SC):
                for to, of in ((dg, d2), (tg, t2)):
                    e.indirect_dma_start(out=to[:, c, :], out_offset=None, in_=of[:, :],
                                         in_offset=bass.IndirectOffsetOnAxis(ap=tki[:, c:c + 1], axis=0)).then_inc(s_g, 16)

        @block.vector
        def _(e):
            done = Chain(e, s_v)
            done(e.memset(on[:, :], 1.0))
            n_ld = 16 * (4 + (2 if REST else 0))
            e.wait_ge(s_ld, n_ld)
            for ri, rf in ((fi, bf), (li, bl)):
                done(e.tensor_scalar(out=ri[:, :], in0=ri[:, :], scalar1=7, scalar2=None, op0=ALU.arith_shift_right))
                done(e.tensor_scalar(out=rf[:, :], in0=ri[:, :], scalar1=float(NB - 1), scalar2=None, op0=ALU.min))
            done(e.scalar_tensor_tensor(out=nn[:, :], in0=bl[:, :], scalar=1.0, in1=bf[:, :], op0=ALU.add, op1=ALU.subtract))
            done(e.tensor_tensor_scan(out=ni[:, :], data0=on[:, :], data1=nn[:, :], initial=0.0, op0=ALU.mult, op1=ALU.add))
            done(e.tensor_tensor(out=N0[:, :], in0=ni[:, :], in1=nn[:, :], op=ALU.subtract))
            done(e.tensor_tensor(out=V[:, :], in0=bf[:, :], in1=N0[:, :], op=ALU.subtract))
            done(e.tensor_copy(dV[:, 0:1], V[:, 0:1]))
            done(e.tensor_tensor(out=dV[:, 1:NT], in0=V[:, 1:NT], in1=V[:, 0:NT - 1], op=ALU.subtract))
            e.sem_inc(s_done, 1)
            e.wait_ge(s_pe, 1)
            for i, (a, n) in enumerate(CH):
                done(e.tensor_copy(Nb[:, a:a + n], ps[i][:, 0:n]))
                done(e.tensor_copy(dVb[:, a:a + n], ps[4 + i][:, 0:n]))
            for c in range(SC):
                done(e.tensor_scalar(out=junk, in0=Nb[:, :], scalar1=A.kcol[:, c:c + 1], scalar2=0.0,
                                     op0=ALU.is_le, op1=ALU.add, accum_out=tk[:, c:c + 1]))
                done(e.scalar_tensor_tensor(out=junk, in0=Nb[:, :], scalar=A.kcol[:, c:c + 1], in1=dVb[:, :],
                                            op0=ALU.is_le, op1=ALU.mult, accum_out=vb[:, c:c + 1]))
            done(e.tensor_scalar(out=tk[:, :], in0=tk[:, :], scalar1=-1.0, scalar2=None, op0=ALU.add))
            done(e.tensor_copy(tki[:, :], tk[:, :]))
            e.sem_inc(s_idx, 1)
            done(e.tensor_tensor(out=bk[:, :], in0=vb[:, :], in1=A.kcol[:, :], op=ALU.add))
            done(e.tensor_scalar(out=bk[:, :], in0=bk[:, :], scalar1=float(NB), scalar2=None, op0=ALU.min))
            done(e.memset(tr[:, :], 0.0))
            for i in range(1, -(-NT // RING)):
                done(e.scalar_tensor_tensor(out=tr[:, :], in0=tk[:, :], scalar=float(i * RING), in1=tr[:, :], op0=ALU.is_ge, op1=ALU.add))
            done(e.scalar_tensor_tensor(out=tr[:, :], in0=tr[:, :], scalar=-float(RING), in1=tk[:, :], op0=ALU.mult, op1=ALU.add))
            done(e.tensor_scalar(out=nb128[:, :], in0=bk[:, :], scalar1=-float(P), scalar2=None, op0=ALU.mult))
            e.sem_inc(s_done, 1)
            e.wait_ge(s_pe, 2)
            done(e.tensor_copy(rowi[:, 0, :], ps[0][0:SC, 0:P]))
            done(e.tensor_copy(rowi[:, 1, :], ps[1][0:SC, 0:P]))
            e.sem_inc(s_rw, 1)
            e.wait_ge(s_row2, 32)
            done(e.memset(brf[:, 0:1], -1.0))
            done(e.tensor_copy(brf[:, 1:NS + 1], A.brow[0:1, :]))
            done(e.tensor_tensor(out=brd[:, :], in0=brf[:, 1:NS + 1], in1=brf[:, 0:NS], op=ALU.is_equal))
            done(e.tensor_copy(df[:, 0:FULL, :], snat[:, 0:FULL, :]))
            done(e.scalar_tensor_tensor(out=tf[:, 0:FULL, :], in0=snat[:, 0:FULL, :], scalar=float(R), in1=tnat[:, 0:FULL, :],
                                        op0=ALU.mult, op1=ALU.add))
            if REST:
                done(e.tensor_copy(df[0:REST, FULL, :], snat[0:REST, FULL, :]))
                done(e.scalar_tensor_tensor(out=tf[0:REST, FULL, :], in0=snat[0:REST, FULL, :], scalar=float(R),
                                            in1=tnat[0:REST, FULL, :], op0=ALU.mult, op1=ALU.add))
            e.sem_inc(s_done, 1)
            k = 2
            for which, to in ((0, ix0), (1, ix1)):
                for c in range(0, FULL + 1, 4):
                    k += 1
                    e.wait_ge(s_pe, k)
                    w = min(NTP - c * P, 4 * P)
                    done(e.tensor_copy(to[:, c * P:c * P + w], ps[k % 2][:, 0:w]))
                    e.sem_inc(s_done, 1)
            for c in range(0, NS, 512):
                k += 1
                e.wait_ge(s_pe, k)
                w = min(NS - c, 512)
                done(e.tensor_copy(contb[:, c:c + w], ps[k % 2][:, 0:w]))
                e.sem_inc(s_done, 1)
            e.wait_ge(s_g, 16 * 2 * SC)
            for c in range(SC):
                done(e.tensor_scalar(out=df[:, c, :], in0=dg[:, c, :], scalar1=nb128[:, c:c + 1], scalar2=None, op0=ALU.add))
            done(e.tensor_copy(tf[:, :, :], tg[:, :, :]))
            e.sem_inc(s_done, 1)
            for which, to in ((0, A.dstl), (1, typ)):
                for c in range(0, SC, 4):
                    k += 1
                    e.wait_ge(s_pe, k)
                    w = min(NS - c * P, 4 * P)
                    done(e.tensor_copy(to[:, c * P:c * P + w], ps[k % 2][:, 0:w]))
                    e.sem_inc(s_done, 1)
            e.sem_inc(s_tab, 1)

        @block.tensor
        def _(e):
            n = [0, 0]

            def done_needed():
                n[0] += 1
                e.wait_ge(s_done, n[0])

            def sent(ins):
                n[1] += 1
                ins.then_inc(s_pe, 1)

            done_needed()
            for i, (a, w) in enumerate(CH):
                e.matmul(ps[i][:, 0:w], A.ones[0:1, :], N0[0:1, a:a + w], start=True, stop=True)
                last = e.matmul(ps[4 + i][:, 0:w], A.ones[0:1, :], dV[0:1, a:a + w], start=True, stop=True)
            sent(last)
            done_needed()
            e.transpose(ps[0][0:SC, 0:P], bk[:, :], A.ident[:, :])
            sent(e.transpose(ps[1][0:SC, 0:P], tr[:, :], A.ident[:, :]))
            done_needed()
            base = n[0]
            k = 2
            first = 3

            def bank():
                nonlocal k
                k += 1
                if k - first >= 2:
                    e.wait_ge(s_done, base + k - first - 1)
                return ps[k % 2]

            for arr in (df, tf):
                for c in range(0, FULL + 1, 4):
                    b = bank()
                    for j in range(c, min(c + 4, FULL + (1 if REST else 0))):
                        rows = P if j < FULL else REST
                        last = e.transpose(b[:, (j - c) * P:(j - c) * P + rows], arr[0:rows, j, :], A.ident[0:rows, 0:rows])
                    sent(last)
            for c in range(0, NS, 512):
                b = bank()
                w = min(NS - c, 512)
                sent(e.matmul(b[:, 0:w], A.ones[0:1, :], brd[0:1, c:c + w], start=True, stop=True))
            e.wait_ge(s_done, base + (k - first + 1) + 1)
            base = base + (k - first + 1) + 1
            first = k + 1
            for arr in (df, tf):
                for c in range(0, SC, 4):
                    b = bank()
                    for j in range(c, min(c + 4, SC)):
                        last = e.transpose(b[:, (j - c) * P:(j - c + 1) * P], arr[:, j, :], A.ident[:, :])
                    sent(last)


def split3(e, done, out3, src, rem, w, n):
    cut = lambda i: out3[:, 0:n, i * w:(i + 1) * w]
    done(e.tensor_copy(cut(0), src))
    done(e.tensor_tensor(out=rem, in0=src, in1=cut(0), op=ALU.subtract))
    done(e.tensor_copy(cut(1), rem))
    done(e.tensor_tensor(out=rem, in0=rem, in1=cut(1), op=ALU.subtract))
    done(e.tensor_copy(cut(2), rem))


def phase_nodes0(nc, A):
    G4 = [(b, min(4, NB - b)) for b in range(0, NB, 4)]
    with ExitStack() as ctx:
        sem = lambda n: ctx.enter_context(nc.semaphore(n))
        sb = lambda n, s, d: ctx.enter_context(nc.sbuf_tensor(n, s, d))
        A32 = sb("A32", [P, NB, D], F32)
        xT = sb("xT", [D + 1, 2, 4, P], F32)
        Bst = sb("B_stage", [P, 2, 4, D], F32)
        pt = [bank(ctx, nc, f"pt{i}", [D, 4, P]) for i in range(2)]
        pa = [bank(ctx, nc, f"pa{i}", [P, O, D]) for i in range(2)]
        pm = [bank(ctx, nc, f"pm{i}", [P, O, D]) for i in range(2)]
        s_pt, s_xt, s_pm, s_a, s_b, s_bd, s_v, s_on = (sem(n) for n in (
            "n0_xt_psum", "n0_xt", "n0_prod", "n0_a", "n0_b", "n0_btab", "n0_dve", "n0_ones"))
        s_bdma = [sem(f"n0_bdma{i}") for i in range(2)]
        block = ctx.enter_context(nc.Block())
        Bv = A.Btab.rearrange("(b p) d -> p b d", p=P)

        @block.tensor
        def _(e):
            e.wait_ge(s_on, 1)
            for g, (b0, n) in enumerate(G4):
                if g >= 2:
                    e.wait_ge(s_xt, g - 1)
                for j in range(n):
                    last = e.transpose(pt[g % 2][:, j, :], A.XA[:, b0 + j, 0:D], A.ident[:, :])
                last.then_inc(s_pt, 1)
                e.wait_ge(s_xt, g + 1)
                if g >= 2:
                    e.wait_ge(s_a, g - 1)
                    e.wait_ge(s_b, g - 1)
                for j in range(n):
                    e.matmul(pa[g % 2][:, j, :], xT[:, g % 2, j, :], A.rhs0[:, 0:D], start=True, stop=True)
                    last = e.matmul(pm[g % 2][:, j, :], xT[:, g % 2, j, :], A.rhs0[:, D:2 * D], start=True, stop=True)
                last.then_inc(s_pm, 1)

        @block.scalar
        def _(e):
            for g, (b0, n) in enumerate(G4):
                e.wait_ge(s_pt, g + 1)
                if g >= 2:
                    e.wait_ge(s_pm, g - 1)
                e.copy(xT[0:D, g % 2, 0:n, :], pt[g % 2][:, 0:n, :]).then_inc(s_xt, 1)
                e.wait_ge(s_pm, g + 1)
                e.copy(A32[:, b0:b0 + n, :], pa[g % 2][:, 0:n, :]).then_inc(s_a, 1)

        @block.vector
        def _(e):
            done = Chain(e, s_v)
            e.memset(xT[D:D + 1, :, :, :], 1.0).then_inc(s_on, 1)
            for g, (b0, n) in enumerate(G4):
                e.wait_ge(s_pm, g + 1)
                if g >= 2:
                    e.wait_ge(s_bdma[g % 2], 16 * (g // 2))
                e.tensor_copy(Bst[:, g % 2, 0:n, :], pm[g % 2][:, 0:n, :]).then_inc(s_b, 1)
            e.wait_ge(s_a, len(G4))
            done(e.memset(A.A3[:, NB:NB + 1, :], 0.0))
            split3(e, done, A.A3, A32[:, :, :], A32[:, :, :], D, NB)

        @block.sync
        def _(e):
            for g, (b0, n) in enumerate(G4):
                e.wait_ge(s_b, g + 1)
                e.dma_start(Bv[:, b0:b0 + n, :], Bst[:, g % 2, 0:n, :]).then_inc(s_bdma[g % 2], 16)
            for i in range(2):
                e.wait_ge(s_bdma[i], 16 * len(range(i, len(G4), 2)))


def drive(e, emit, last_lag):
    static = lambda s: emit(s, s % Q, s // Q, lambda lag: 0 <= s - lag < SO, lambda ahead: s + ahead < TO)
    first = -(-last_lag // Q)
    last = TO // Q - 1
    for s in range(first * Q):
        static(s)
    on = lambda x: True
    with e.Fori(first, last) as turn:
        for q in range(Q):
            emit(turn * Q + q, q, turn, on, on)
    for s in range(last * Q, SO + last_lag):
        static(s)


def weave(*streams):
    streams = list(streams)
    while streams:
        for g in list(streams):
            if next(g, streams) is streams:
                streams.remove(g)


def load_regs(e, regs, row, s):
    e.reg_load(regs, row[0:1, bass.ds(s * O, O)])


def phase_layer0(nc, A):
    with ExitStack() as ctx:
        sem = lambda n: ctx.enter_context(nc.semaphore(n))
        sb = lambda n, s, d: ctx.enter_context(nc.sbuf_tensor(n, s, d))
        pb = lambda n, s: bank(ctx, nc, n, s)
        ring = sb("ring0", [P, RING, D], F32)
        OH = sb("oh0", [P, Q, O, P], F32)
        OHT = sb("oht0", [P, Q, O, P], BF16)
        G = sb("g0", [P, Q, O, D], F32)
        idx = sb("idx0", [P, NTP], I32)
        ir = sb("ir0", [P, Q, O], I32)
        msg = sb("msg", [P, 2, O, D], F32)
        ea = sb("ea", [P, Q, O, DE], F32)
        eaT = sb("eaT", [P, 2, 2, P], F32)
        pT = [pb(f"p0_t{h}", [P, 4, P]) for h in range(2)]
        pE = pb("p0_ea", [P, 2, P])
        pC = pb("p0_c", [P, O, D])
        pM = pb("p0_m", [P, O, D])
        pS = pb("p0_s", [P, O, D])
        names = ("oh_full oh_free t_full0 t_full1 oht_full oht_free ea_full ea_free eap_full eap_free "
                 "eat_full c_full c_free base_full ring_free m_full msg_full msg_free s_full s_free "
                 "g_free ir_full dve").split()
        S = {n: sem("l0_" + n) for n in names}
        s_g = [sem(f"l0_g{q}") for q in range(Q)]
        s_ea = [sem(f"l0_ea{q}") for q in range(Q)]
        s_ix = sem("l0_ix")
        block = ctx.enter_context(nc.Block())
        eav = A.ea_in.rearrange("(t p) f -> p t f", p=P)
        eas = A.ea_s.rearrange("(t p) f -> p t f", p=P)

        @block.sync
        def _(e):
            e.dma_start(idx[:, :], A.ix0_d).then_inc(s_ix, 16)
            e.sem_inc(S["ea_free"], Q)
            bad = descends(e, A, "l0_sp")

            def emit(s, q, turn, on, tile):
                if tile(0):
                    take(e, S["ea_free"])
                    with e.If(bad == 0):
                        e.dma_start(ea[:, q, :, :], eav[:, bass.ds(s * O, O), :]).then_inc(s_ea[q], 16)
                    with e.Else():
                        e.dma_start(ea[:, q, :, :], eas[:, bass.ds(s * O, O), :]).then_inc(s_ea[q], 16)
            drive(e, emit, 0)

        @block.gpsimd
        def _(e):
            def emit(s, q, turn, on, tile):
                if tile(0):
                    take(e, S["ir_full"])
                    for j in range(O):
                        e.indirect_dma_start(out=G[:, q, j, :], out_offset=None, in_=A.Btab[:, :],
                                             in_offset=bass.IndirectOffsetOnAxis(ap=ir[:, q, j:j + 1], axis=0)).then_inc(s_g[q], 16)
            drive(e, emit, 0)

        @block.scalar
        def _(e):
            e.wait_ge(s_ix, 16)
            for q in range(Q):
                e.copy(ir[:, q, :], idx[:, q * O:(q + 1) * O]).then_inc(S["ir_full"], 1)
            e.sem_inc(S["oht_free"], Q)
            e.sem_inc(S["msg_free"], 2)

            def emit(s, q, turn, on, tile):
                if on(3):
                    take(e, S["m_full"])
                    take(e, S["msg_free"])
                    e.activation(msg[:, (q - 3) % 2, :, :], pM[:, :, :], ACT.Relu).then_inc(S["msg_full"], 1)
                if tile(0):
                    take(e, S["eap_full"])
                    e.copy(eaT[:, q % 2, :, :], pE[:, :, :]).then_inc(S["eat_full"], 1)
                if on(1):
                    take(e, S["oht_free"])
                    for h in range(2):
                        take(e, S[f"t_full{h}"])
                        e.copy(OHT[:, (q - 1) % Q, 4 * h:4 * h + 4, :], pT[h][:, :, :]).then_inc(S["oht_full"], 1)
                if on(1) and tile(Q - 1):
                    take(e, S["g_free"])
                    e.copy(ir[:, (q - 1) % Q, :], idx[:, bass.ds((s + Q - 1) * O, O)]).then_inc(S["ir_full"], 1)
            drive(e, emit, 3)

        @block.tensor
        def _(e):
            breg = [e.alloc_register(f"l0pb{j}") for j in range(O)]
            treg = [e.alloc_register(f"l0pt{j}") for j in range(O)]
            e.sem_inc(S["oh_free"], Q)

            def emit(s, q, turn, on, tile):
                if tile(0):
                    e.wait_ge(s_ea[q], 16 * turn + 16)
                if on(1) and tile(-1):
                    take(e, S["eat_full"])
                    e.sem_inc(S["ea_free"], 1)
                if tile(0):
                    for h in range(2):
                        last = e.transpose(pE[:, h, :], ea[:, q, 4 * h:4 * h + 4, :].rearrange("p t f -> p (t f)"), A.ident[:, :])
                    last.then_inc(S["eap_full"], 1)
                if on(2):
                    take(e, S["oht_full"], 2)
                if on(1):
                    take(e, S["oh_full"])
                    for h in range(2):
                        for j in range(4):
                            last = e.transpose(pT[h][:, j, :], OH[:, (q - 1) % Q, 4 * h + j, :], A.ident[:, :])
                        last.then_inc(S[f"t_full{h}"], 1)
                if on(1) and tile(-1):
                    take(e, S["c_free"])
                    for h in range(2):
                        last = e.matmul(pC[:, 4 * h:4 * h + 4, :], eaT[:, (q - 1) % 2, h, :], A.W1c4[:, :], start=True, stop=True)
                    last.then_inc(S["c_full"], 1)
                if on(3):
                    take(e, S["msg_full"])
                if on(2):
                    load_regs(e, breg, A.brow, s - 2)
                    load_regs(e, treg, A.trow, s - 2)
                    if tile(-2):
                        take(e, S["base_full"])
                    for j in range(O):
                        b = e.snap(breg[j], min_val=0, max_val=NB)
                        t = e.snap(treg[j], min_val=0, max_val=RING - 1)
                        for part in range(3):
                            e.matmul(pM[:, j, :], OHT[:, (q - 2) % Q, j, :], A.A3[:, bass.ds(b, 1), part * D:(part + 1) * D],
                                     start=(part == 0), stop=False)
                        last = e.matmul(pM[:, j, :], A.ident[:, :], ring[:, bass.ds(t, 1), :], start=False, stop=True)
                    last.then_inc(S["m_full"], 1)
                if on(3):
                    e.sem_inc(S["oht_free"], 1)
                    e.sem_inc(S["ring_free"], 1)
                    take(e, S["s_free"])
                    for j in range(O):
                        last = e.matmul(pS[:, j, :], OH[:, (q - 3) % Q, j, :], msg[:, (q - 3) % 2, j, :], start=True, stop=True)
                    last.then_inc(S["s_full"], 1)
            drive(e, emit, 3)

        @block.vector
        def _(e):
            done = Chain(e, S["dve"])
            breg = [e.alloc_register(f"l0vb{j}") for j in range(O)]
            e.sem_inc(S["c_free"], 1)
            e.sem_inc(S["s_free"], 1)
            e.sem_inc(S["ring_free"], LEAD)

            def emit(s, q, turn, on, tile):
                if on(4):
                    load_regs(e, breg, A.brow, s - 4)
                    take(e, S["s_full"])
                    e.sem_inc(S["oh_free"], 1)
                    e.sem_inc(S["msg_free"], 1)
                    for j in range(O):
                        b = e.snap(breg[j], min_val=0, max_val=NB)
                        acc = A.XA[:, bass.ds(b, 1), D:2 * D]
                        done(e.tensor_tensor(out=acc, in0=acc, in1=pS[:, j:j + 1, :], op=ALU.add))
                    e.sem_inc(S["s_free"], 1)
                if on(0):
                    take(e, S["oh_free"])
                    e.tensor_tensor(out=OH[:, q, :, :], in0=A.iota[:, :].unsqueeze(1).to_broadcast([P, O, P]),
                                    in1=A.dstl[:, bass.ds(s * O, O)].unsqueeze(2).to_broadcast([P, O, P]),
                                    op=ALU.is_equal).then_inc(S["oh_full"], 1)
                if on(1) and tile(-1):
                    r = (q - 1) % Q
                    n = turn if q else turn - 1
                    e.wait_ge(s_g[r], 16 * O * n + 16 * O)
                    take(e, S["c_full"])
                    take(e, S["ring_free"])
                    done(e.tensor_tensor(out=ring[:, bass.ds(((s - 1) * O) % RING, O), :], in0=G[:, r, :, :], in1=pC[:, :, :], op=ALU.add))
                    e.sem_inc(S["base_full"], 1)
                    e.sem_inc(S["c_free"], 1)
                    e.sem_inc(S["g_free"], 1)
            drive(e, emit, 4)


def layernorm(e, act_sqrt, done, y, x2, st, n):
    mean, var = st
    done(e.tensor_reduce(out=mean, in_=y, axis=AXX, op=ALU.add))
    done(e.tensor_scalar(out=mean, in0=mean, scalar1=1.0 / D, scalar2=None, op0=ALU.mult))
    done(e.tensor_tensor(out=y, in0=y, in1=mean.unsqueeze(2).to_broadcast([P, n, D]), op=ALU.subtract))
    done(e.tensor_tensor(out=x2, in0=y, in1=y, op=ALU.mult))
    done(e.tensor_reduce(out=var, in_=x2, axis=AXX, op=ALU.add))
    act_sqrt()
    done(e.reciprocal(out=var, in_=var))
    done(e.tensor_tensor(out=x2, in0=y, in1=var.unsqueeze(2).to_broadcast([P, n, D]), op=ALU.mult))


def phase_mid(nc, A):
    G4 = [(b, min(4, NB - b)) for b in range(0, NB, 4)]
    LNB = 14
    assert NB % LNB == 0
    with ExitStack() as ctx:
        sem = lambda n: ctx.enter_context(nc.semaphore(n))
        sb = lambda n, s, d: ctx.enter_context(nc.sbuf_tensor(n, s, d))
        Y = sb("Y", [P, NB, D], F32)
        xaT = sb("xaT", [P, 2, 4, P], F32)
        x1T = sb("x1T", [D + 1, 2, 4, P], F32)
        Zst = sb("Z_stage", [P, 4, R * ZW], F32)
        S2 = sb("S2", [P, NB, R], F32)
        mean = sb("mean", [P, LNB], F32)
        var = sb("var", [P, LNB], F32)
        pt = [bank(ctx, nc, f"q_t{i}", [P, 4, P]) for i in range(2)]
        pm = [bank(ctx, nc, f"q_h{i}", [P, 4, D]) for i in range(2)]
        pz = [bank(ctx, nc, f"q_z{i}", [P, 512]) for i in range(4)]
        s_pt, s_xt, s_h, s_y, s_v, s_on, s_sq, s_sd, s_x1, s_pt1, s_x1t, s_z0, s_zv, s_za = (sem("mid_" + n) for n in (
            "pt xt h y dve ones sqrt_in sqrt_out x1 pt1 x1t z zv za").split())
        s_zd = [sem(f"mid_zd{i}") for i in range(4)]
        block = ctx.enter_context(nc.Block())
        Zv = A.Ztab.rearrange("(b p r) c -> p b (r c)", p=P, r=R)
        HALF = R * ZW // 2

        @block.tensor
        def _(e):
            for g, (b0, n) in enumerate(G4):
                if g >= 2:
                    e.wait_ge(s_xt, g - 1)
                for j in range(n):
                    last = e.transpose(pt[g % 2][:, j, :], A.XA[:, b0 + j, 0:2 * D], A.ident[:, :])
                last.then_inc(s_pt, 1)
                e.wait_ge(s_xt, g + 1)
                if g >= 2:
                    e.wait_ge(s_y, g - 1)
                for j in range(n):
                    e.matmul(pm[g % 2][:, j, :], xaT[:, g % 2, j, :], A.W2ab[:, :], start=True, stop=False)
                    last = e.matmul(pm[g % 2][:, j, :], A.ones[0:1, :], A.b2row[0:1, :], start=False, stop=True)
                last.then_inc(s_h, 1)
            e.wait_ge(s_on, 1)
            for g, (b0, n) in enumerate(G4):
                e.wait_ge(s_x1, -(-(b0 + n) // LNB))
                if g >= 2:
                    e.wait_ge(s_x1t, g - 1)
                for j in range(n):
                    last = e.transpose(pt[g % 2][0:D, j, :], A.x1[:, b0 + j, :], A.ident[:, :])
                last.then_inc(s_pt1, 1)
                e.wait_ge(s_x1t, g + 1)
                for j in range(n):
                    b = b0 + j
                    if b >= 2:
                        e.wait_ge(s_zv, b - 1)
                        e.wait_ge(s_za, b - 1)
                    e.matmul(pz[2 * (b % 2)][:, 0:HALF], x1T[:, g % 2, j, :], A.rhs1[:, 0:HALF], start=True, stop=True)
                    e.matmul(pz[2 * (b % 2) + 1][:, 0:HALF + R], x1T[:, g % 2, j, :], A.rhs1[:, HALF:2 * HALF + R],
                             start=True, stop=True).then_inc(s_z0, 1)

        @block.scalar
        def _(e):
            for g, (b0, n) in enumerate(G4):
                e.wait_ge(s_pt, g + 1)
                if g >= 2:
                    e.wait_ge(s_h, g - 1)
                e.copy(xaT[:, g % 2, 0:n, :], pt[g % 2][:, 0:n, :]).then_inc(s_xt, 1)
            k = 0

            def root():
                nonlocal k
                k += 1
                e.wait_ge(s_sq, k)
                e.activation(var[:, :], var[:, :], ACT.Sqrt, scale=1.0 / D, bias=A.epsb[:, 0:1]).then_inc(s_sd, 1)
            for i in range(NB // LNB):
                root()
            for g, (b0, n) in enumerate(G4):
                e.wait_ge(s_pt1, g + 1)
                if g >= 2:
                    e.wait_ge(s_z0, 4 * (g - 1))
                e.copy(x1T[0:D, g % 2, 0:n, :], pt[g % 2][0:D, 0:n, :]).then_inc(s_x1t, 1)
                for j in range(n):
                    b = b0 + j
                    e.wait_ge(s_z0, b + 1)
                    if b >= 4:
                        e.wait_ge(s_zd[b % 4], 16 * (b // 4))
                    e.copy(S2[:, b, :], pz[2 * (b % 2) + 1][:, HALF:HALF + R])
                    e.copy(Zst[:, b % 4, HALF:2 * HALF], pz[2 * (b % 2) + 1][:, 0:HALF]).then_inc(s_za, 1)

        @block.vector
        def _(e):
            done = Chain(e, s_v)
            e.memset(x1T[D:D + 1, :, :, :], 1.0).then_inc(s_on, 1)
            for g, (b0, n) in enumerate(G4):
                e.wait_ge(s_h, g + 1)
                e.scalar_tensor_tensor(out=Y[:, b0:b0 + n, :], in0=pm[g % 2][:, 0:n, :], scalar=0.0,
                                       in1=A.XA[:, b0:b0 + n, 0:D], op0=ALU.max, op1=ALU.add).then_inc(s_y, 1)
            e.wait_ge(s_y, len(G4))
            for i in range(NB // LNB):
                def root():
                    e.sem_inc(s_sq, 1)
                    e.wait_ge(s_sd, i + 1)
                sl = slice(i * LNB, (i + 1) * LNB)
                layernorm(e, root, done, Y[:, sl, :], A.x1[:, sl, :], (mean[:, :], var[:, :]), LNB)
                e.sem_inc(s_x1, 1)
            for b in range(NB):
                e.wait_ge(s_z0, b + 1)
                if b >= 4:
                    e.wait_ge(s_zd[b % 4], 16 * (b // 4))
                done(e.tensor_copy(Zst[:, b % 4, 0:HALF], pz[2 * (b % 2)][:, 0:HALF]))
                e.sem_inc(s_zv, 1)
            done(e.memset(A.S23[:, NB:NB + 1, :], 0.0))
            e.wait_ge(s_za, NB)
            split3(e, done, A.S23, S2[:, :, :], S2[:, :, :], R, NB)

        @block.sync
        def _(e):
            for b in range(NB):
                e.wait_ge(s_zv, b + 1)
                e.wait_ge(s_za, b + 1)
                e.dma_start(Zv[:, b, :], Zst[:, b % 4, :]).then_inc(s_zd[b % 4], 16)
            for i in range(4):
                e.wait_ge(s_zd[i], 16 * len(range(i, NB, 4)))


def phase_layer1(nc, A):
    with ExitStack() as ctx:
        sem = lambda n: ctx.enter_context(nc.semaphore(n))
        sb = lambda n, s, d: ctx.enter_context(nc.sbuf_tensor(n, s, d))
        pb = lambda n, s: bank(ctx, nc, n, s)
        ring = sb("ring1", [P, RING, ZW], F32)
        OH = sb("oh1", [P, Q, O, P], F32)
        OHT = sb("oht1", [P, Q, O, P], BF16)
        OHe = sb("ohe", [P, 2, O, P], F32)
        OHx = sb("ohx", [P, 2, O, P], F32)
        G = sb("g1", [P, Q, O, ZW], F32)
        idx = sb("idx1", [P, NTP], I32)
        ir = sb("ir1", [P, Q, O], I32)
        typ = sb("typ1", [P, NS], F32)
        cont = sb("cont1", [P, NS], F32)
        TY = sb("ty", [P, O, R], F32)
        pr = sb("prod", [P, O, 3 * R], F32)
        ev = sb("ev", [P, Q, O], F32)
        ms = sb("mslot", [P, O], F32)
        mr = sb("mrun", [P, Q * O + 1], F32)
        m3 = sb("m3", [P, 2, O, 3], BF16)
        rem = sb("mrem", [P, O], F32)
        fd = sb("fd", [P, Q, O], F32)
        ff = sb("ff", [P, Q, O], F32)
        md = sb("md", [P, O], F32)
        ed = sb("ed", [P, 2, O], F32)
        ex = sb("ex", [P, 2, O], F32)
        pT = [pb(f"p1_t{h}", [P, 4, P]) for h in range(2)]
        pX = [pb(f"p1_x{h}", [P, 4, P]) for h in range(2)]
        pE = pb("p1_e", [P, O, 3 * R])
        pB = pb("p1_b", [P, O, 3])
        pS = [pb(f"p1_s{h}", [P, 4, D + 1]) for h in range(2)]
        names = ("oh_full oh_free t_full0 t_full1 oht_full "
                 "ring_full ring_free e_full e_used ohe_full ohe_free x_full0 x_full1 x_free0 x_free1 m3_full b_full b_free "
                 "fd_full ed_full ex_done ff_full ohx_full ohx_free s_full s_free "
                 "ir_full dve acc fdm ty act").split()
        S = {n: sem("l1_" + n) for n in names}
        s_g = [sem(f"l1_g{q}") for q in range(Q)]
        s_ix = sem("l1_ix")
        block = ctx.enter_context(nc.Block())

        @block.sync
        def _(e):
            e.dma_start(idx[:, :], A.ix1_d).then_inc(s_ix, 16)
            e.dma_start(typ[:, :], A.typ_d).then_inc(s_ix, 16)
            e.dma_start(cont[:, :], A.cont_d).then_inc(s_ix, 16)
            e.wait_ge(s_ix, 48)

        @block.gpsimd
        def _(e):
            def emit(s, q, turn, on, tile):
                if tile(0):
                    take(e, S["ir_full"])
                    for j in range(O):
                        e.indirect_dma_start(out=G[:, q, j, :], out_offset=None, in_=A.Ztab[:, :],
                                             in_offset=bass.IndirectOffsetOnAxis(ap=ir[:, q, j:j + 1], axis=0)).then_inc(s_g[q], 16)
            drive(e, emit, 0)

        @block.scalar
        def _(e):
            done = Chain(e, S["act"])
            e.wait_ge(s_ix, 48)
            for q in range(Q):
                e.copy(ir[:, q, :], idx[:, q * O:(q + 1) * O]).then_inc(S["ir_full"], 1)
            e.sem_inc(S["ring_free"], LEAD)

            def emit(s, q, turn, on, tile):
                if on(4):
                    r, o = (q - 4) % Q, q % 2
                    take(e, S["fd_full"])
                    e.activation(ff[:, r, :], fd[:, r, :], ACT.Exp).then_inc(S["ff_full"], 1)
                    take(e, S["ed_full"])
                    done(e.activation(ex[:, o, :], ed[:, o, :], ACT.Exp))
                    take(e, S["ohx_free"])
                    for j in range(O):
                        ins = e.activation(OHx[:, o, j, :], OH[:, r, j, :], ACT.Copy, scale=ex[:, o, j:j + 1])
                    done(ins)
                    e.sem_inc(S["ohx_full"], 1)
                    e.sem_inc(S["oh_free"], 1)
                if on(1):
                    for h in range(2):
                        take(e, S[f"t_full{h}"])
                        e.copy(OHT[:, (q - 1) % Q, 4 * h:4 * h + 4, :], pT[h][:, :, :]).then_inc(S["oht_full"], 1)
                if tile(0):
                    take(e, S["ring_free"])
                    e.wait_ge(s_g[q], 16 * O * turn + 16 * O)
                    done(e.copy(ring[:, bass.ds((s * O) % RING, O), :], G[:, q, :, :]))
                    e.sem_inc(S["ring_full"], 1)
                    if tile(Q):
                        e.copy(ir[:, q, :], idx[:, bass.ds((s + Q) * O, O)]).then_inc(S["ir_full"], 1)
            drive(e, emit, 4)

        @block.tensor
        def _(e):
            breg = [e.alloc_register(f"l1pb{j}") for j in range(O)]
            treg = [e.alloc_register(f"l1pt{j}") for j in range(O)]
            e.sem_inc(S["oh_free"], Q)
            e.sem_inc(S["ohx_free"], 2)
            e.sem_inc(S["ohe_free"], 2)

            def emit(s, q, turn, on, tile):
                if on(3):
                    take(e, S["ohe_full"])
                    for h in range(2):
                        take(e, S[f"x_free{h}"])
                        for j in range(4):
                            last = e.transpose(pX[h][:, j, :], OHe[:, (q - 3) % 2, 4 * h + j, :], A.ident[:, :])
                        last.then_inc(S[f"x_full{h}"], 1)
                if on(2):
                    take(e, S["oht_full"], 2)
                if on(1):
                    take(e, S["oh_full"])
                    for h in range(2):
                        for j in range(4):
                            last = e.transpose(pT[h][:, j, :], OH[:, (q - 1) % Q, 4 * h + j, :], A.ident[:, :])
                        last.then_inc(S[f"t_full{h}"], 1)
                if on(2):
                    load_regs(e, breg, A.brow, s - 2)
                    load_regs(e, treg, A.trow, s - 2)
                    if tile(-2):
                        take(e, S["ring_full"])
                    take(e, S["e_used"])
                    for j in range(O):
                        b = e.snap(breg[j], min_val=0, max_val=NB)
                        t = e.snap(treg[j], min_val=0, max_val=RING - 1)
                        e.matmul(pE[:, j, :], OHT[:, (q - 2) % Q, j, :], A.S23[:, bass.ds(b, 1), :], start=True, stop=False)
                        last = e.matmul(pE[:, j, 0:R], A.ident[:, :], ring[:, bass.ds(t, 1), D + 1:D + 2].to_broadcast([P, 1, R]),
                                        start=False, stop=True)
                    last.then_inc(S["e_full"], 1)
                if on(3):
                    take(e, S["m3_full"])
                    e.sem_inc(S["ohe_free"], 1)
                    take(e, S["b_free"])
                    for j in range(O):
                        last = e.matmul(pB[:, j, :], OHT[:, (q - 3) % Q, j, :], m3[:, (q - 3) % 2, j, :], start=True, stop=True)
                    last.then_inc(S["b_full"], 1)
                if on(4):
                    load_regs(e, treg, A.trow, s - 4)
                    take(e, S["ohx_full"])
                    take(e, S["s_free"])
                    for j in range(O):
                        t = e.snap(treg[j], min_val=0, max_val=RING - 1)
                        last = e.matmul(pS[j // 4][:, j % 4, :], OHx[:, q % 2, j, :], ring[:, bass.ds(t, 1), 0:D + 1], start=True, stop=True)
                    last.then_inc(S["s_full"], 1)
            e.sem_inc(S["b_free"], 1)
            e.sem_inc(S["s_free"], 1)
            e.sem_inc(S["e_used"], 1)
            for h in range(2):
                e.sem_inc(S[f"x_free{h}"], 1)
            drive(e, emit, 4)

        @block.vector
        def _(e):
            done = Chain(e, S["dve"])
            breg = [e.alloc_register(f"l1vb{j}") for j in range(O)]
            e.wait_ge(s_ix, 48)
            done(e.memset(mr[:, :], 0.0))
            done(e.memset(A.acc1[:, :, :], 0.0))

            def emit(s, q, turn, on, tile):
                weave(sums(s, q, on), scores(s, q, on))

            def sums(s, q, on):
                if on(2):
                    e.tensor_tensor(out=TY[:, :, :], in0=A.iota[:, 0:R].unsqueeze(1).to_broadcast([P, O, R]),
                                    in1=typ[:, bass.ds((s - 2) * O, O)].unsqueeze(2).to_broadcast([P, O, R]),
                                    op=ALU.is_equal).then_inc(S["ty"], 1)
                    yield
                if on(5):
                    load_regs(e, breg, A.brow, s - 5)
                    take(e, S["ff_full"])
                    take(e, S["s_full"])
                    e.sem_inc(S["ohx_free"], 1)
                    e.sem_inc(S["ring_free"], 1)
                    for j in range(O):
                        b = e.snap(breg[j], min_val=0, max_val=NB)
                        acc = A.acc1[:, bass.ds(b, 1), :]
                        if j:
                            take(e, S["acc"])
                        e.scalar_tensor_tensor(out=acc, in0=acc, scalar=ff[:, (q - 5) % Q, j:j + 1],
                                               in1=pS[j // 4][:, j % 4:j % 4 + 1, :], op0=ALU.mult, op1=ALU.add).then_inc(S["acc"], 1)
                        yield
                if on(0):
                    take(e, S["oh_free"])
                    e.tensor_tensor(out=OH[:, q, :, :], in0=A.iota[:, :].unsqueeze(1).to_broadcast([P, O, P]),
                                    in1=A.dstl[:, bass.ds(s * O, O)].unsqueeze(2).to_broadcast([P, O, P]),
                                    op=ALU.is_equal).then_inc(S["oh_full"], 1)
                    yield
                if on(5):
                    take(e, S["acc"])
                    e.sem_inc(S["s_free"], 1)

            def scores(s, q, on):
                after = lambda: take(e, S["dve"])
                if on(3):
                    r = (q - 3) % Q
                    run, last = mr[:, r * O + 1:(r + 1) * O + 1], mr[:, r * O:(r + 1) * O]
                    part = lambda i: m3[:, (q - 3) % 2, :, i:i + 1]
                    if r == 0:
                        e.tensor_copy(mr[:, 0:1], mr[:, Q * O:Q * O + 1])
                    for h in range(2):
                        take(e, S[f"x_full{h}"])
                        e.tensor_reduce(out=ms[:, 4 * h:4 * h + 4], in_=pX[h][:, :, :], axis=AXX, op=ALU.max).then_inc(S["dve"], 1)
                        yield
                        after()
                        e.sem_inc(S[f"x_free{h}"], 1)
                    e.tensor_tensor_scan(out=run, data0=cont[:, bass.ds((s - 3) * O, O)], data1=ms[:, :], initial=mr[:, r * O:r * O + 1],
                                         op0=ALU.mult, op1=ALU.max).then_inc(S["dve"], 1)
                    yield
                    after()
                    e.tensor_copy(part(0), run.unsqueeze(2)).then_inc(S["dve"], 1)
                    e.tensor_tensor(out=fd[:, r, :], in0=last, in1=cont[:, bass.ds((s - 3) * O, O)], op=ALU.mult).then_inc(S["fdm"], 1)
                    yield
                    after()
                    e.tensor_tensor(out=rem[:, :].unsqueeze(2), in0=run.unsqueeze(2), in1=part(0), op=ALU.subtract).then_inc(S["dve"], 1)
                    take(e, S["fdm"])
                    e.tensor_tensor(out=fd[:, r, :], in0=fd[:, r, :], in1=run, op=ALU.subtract).then_inc(S["fd_full"], 1)
                    yield
                    after()
                    e.tensor_copy(part(1), rem[:, :].unsqueeze(2)).then_inc(S["dve"], 1)
                    yield
                    after()
                    e.tensor_tensor(out=part(2), in0=rem[:, :].unsqueeze(2), in1=part(1), op=ALU.subtract).then_inc(S["m3_full"], 1)
                    yield
                if on(2):
                    r = (q - 2) % Q
                    take(e, S["ty"])
                    take(e, S["e_full"])
                    e.tensor_tensor(out=pr[:, :, :].rearrange("p s (a r) -> p s a r", r=R),
                                    in0=pE[:, :, :].rearrange("p s (a r) -> p s a r", r=R),
                                    in1=TY[:, :, :].unsqueeze(2).to_broadcast([P, O, 3, R]), op=ALU.mult).then_inc(S["dve"], 1)
                    yield
                    after()
                    e.sem_inc(S["e_used"], 1)
                    e.tensor_reduce(out=ev[:, r, :], in_=pr[:, :, :], axis=AXX, op=ALU.add).then_inc(S["dve"], 1)
                    yield
                    after()
                    take(e, S["ohe_free"])
                    e.scalar_tensor_tensor(out=OHe[:, (q - 2) % 2, :, :], in0=ev[:, r, :].unsqueeze(2).to_broadcast([P, O, P]), scalar=0.0,
                                           in1=OH[:, r, :, :], op0=ALU.max, op1=ALU.mult).then_inc(S["ohe_full"], 1)
                    yield
                if on(3):
                    r = (q - 3) % Q
                    take(e, S["b_full"])
                    e.tensor_reduce(out=md[:, :], in_=pB[:, :, :], axis=AXX, op=ALU.add).then_inc(S["dve"], 1)
                    yield
                    after()
                    e.sem_inc(S["b_free"], 1)
                    e.scalar_tensor_tensor(out=ed[:, (q - 3) % 2, :], in0=ev[:, r, :], scalar=0.0, in1=md[:, :],
                                           op0=ALU.max, op1=ALU.subtract).then_inc(S["ed_full"], 1)
                    yield
            drive(e, emit, 5)


def phase_out(nc, A):
    LNB = 14
    with ExitStack() as ctx:
        sem = lambda n: ctx.enter_context(nc.semaphore(n))
        sb = lambda n, s, d: ctx.enter_context(nc.sbuf_tensor(n, s, d))
        Y = sb("Yo", [P, NB, D], F32)
        den = sb("den", [P, NB, 1], F32)
        mean = sb("mean_o", [P, LNB], F32)
        var = sb("var_o", [P, LNB], F32)
        s_v, s_sq, s_sd, s_o, s_od = (sem("out_" + n) for n in ("dve", "sq", "sd", "ready", "dma"))
        block = ctx.enter_context(nc.Block())
        LAST = N - (NB - 1) * P

        @block.vector
        def _(e):
            done = Chain(e, s_v)
            done(e.tensor_scalar(out=den[:, :, :], in0=A.acc1[:, 0:NB, D:D + 1], scalar1=1e-20, scalar2=None, op0=ALU.max))
            done(e.reciprocal(out=den[:, :, :], in_=den[:, :, :]))
            for i in range(NB // LNB):
                def root():
                    e.sem_inc(s_sq, 1)
                    e.wait_ge(s_sd, i + 1)
                sl = slice(i * LNB, (i + 1) * LNB)
                done(e.tensor_tensor(out=Y[:, sl, :], in0=A.acc1[:, sl, 0:D], in1=den[:, sl, :].to_broadcast([P, LNB, D]), op=ALU.mult))
                done(e.tensor_tensor(out=Y[:, sl, :], in0=Y[:, sl, :], in1=A.x1[:, sl, :], op=ALU.add))
                layernorm(e, root, done, Y[:, sl, :], A.x1[:, sl, :], (mean[:, :], var[:, :]), LNB)
                e.sem_inc(s_o, 1)

        @block.scalar
        def _(e):
            for i in range(NB // LNB):
                e.wait_ge(s_sq, i + 1)
                e.activation(var[:, :], var[:, :], ACT.Sqrt, scale=1.0 / D, bias=A.epsb[:, 0:1]).then_inc(s_sd, 1)

        @block.sync
        def _(e):
            ov = A.out[0:(NB - 1) * P, :].rearrange("(b p) d -> p b d", p=P)
            for i in range(NB // LNB):
                e.wait_ge(s_o, i + 1)
                hi = min((i + 1) * LNB, NB - 1)
                e.dma_start(ov[:, i * LNB:hi, :], A.x1[:, i * LNB:hi, :]).then_inc(s_od, 16)
            e.dma_start(A.out[(NB - 1) * P:N, :], A.x1[0:LAST, NB - 1, :]).then_inc(s_od, 16)
            e.wait_ge(s_od, 16 * (NB // LNB + 1))


class Arrays:
    pass


def build(nc, A):
    with ExitStack() as ctx:
        sb = lambda n, s, d, c=ctx: c.enter_context(nc.sbuf_tensor(n, s, d))
        A.ident = sb("ident", [P, P], F32)
        A.iota = sb("iota", [P, P], F32)
        A.kcol = sb("kcol", [P, SC], F32)
        A.ones = sb("ones", [P, P], F32)
        A.epsb = sb("epsb", [P, 1], F32)
        A.rhs0 = sb("rhs0", [D + 1, 2 * D], F32)
        A.rhs1 = sb("rhs1", [D + 1, R * ZW + R], F32)
        A.W2ab = sb("W2ab", [P, D], F32)
        A.W1c4 = sb("W1c4", [P, 4 * D], F32)
        A.b2row = sb("b2row", [1, D], F32)
        A.or_col = sb("or_col", [P, 3], I32)
        A.flag = sb("flag", [1, 1], I32)
        A.brow = sb("brow", [1, NS], I32)
        A.trow = sb("trow", [1, NS], I32)
        A.dstl = sb("dstl", [P, NS], F32)
        A.S23 = sb("S23", [P, NB + 1, 3 * R], BF16)
        A.XA = sb("XA", [P, NB + 1, 2 * D + 1], F32)
        A.x1 = A.XA[:, 0:NB, 0:D]
        A.acc1 = A.XA[:, :, D:2 * D + 1]
        phase_inputs(nc, A)
        phase_order(nc, A)
        phase_slots(nc, A)
        with ExitStack() as c1:
            A.A3 = sb("A3", [P, NB + 1, 3 * D], BF16, c1)
            phase_nodes0(nc, A)
            phase_layer0(nc, A)
        phase_mid(nc, A)
        phase_layer1(nc, A)
        phase_out(nc, A)


def kernel(**inputs):
    import numpy as np
    import concourse.bacc as bacc
    from concourse.bass_utils import run_bass_kernel_spmd as run

    nc = bacc.Bacc("TRN2", target_bir_lowering=False, num_devices=1)
    A = Arrays()
    feed = {}

    def give(attr, a, dt):
        a = np.ascontiguousarray(a)
        feed["in_" + attr] = a
        setattr_ = A.__dict__
        setattr_[attr] = nc.dram_tensor("in_" + attr, a.shape, dt, kind="ExternalInput").ap()

    def padded(a, n, fill=0):
        a = np.asarray(a)
        out = np.full((n,) + a.shape[1:], fill, a.dtype)
        out[:a.shape[0]] = a
        return out

    give("x_in", padded(inputs["x"], NP), F32)
    give("dst_in", padded(inputs["dst"], EP + 1, DST_PAD), I32)
    give("src_in", padded(inputs["src"], EP), I32)
    give("typ_in", padded(inputs["edge_type_8"], EP), I32)
    give("ea_in", padded(inputs["edge_attr_32"], EP), F32)
    give("u_in", inputs["L0_gnn_u"], F32)
    give("W1_in", inputs["L0_gnn_W1"], F32)
    give("b1_in", inputs["L0_gnn_b1"], F32)
    give("W2_in", inputs["L0_gnn_W2"], F32)
    give("b2_in", inputs["L0_gnn_b2"], F32)
    give("fc_in", inputs["L1_gnn_fc_weight"], F32)
    give("aw_in", inputs["L1_gnn_attn_weight"], F32)
    dr = lambda n, s, d: nc.dram_tensor(n, s, d, kind="Internal").ap()
    A.dst_s = dr("dst_s", (NTP, P), I32)
    A.src_s = dr("src_s", (NTP, P), I32)
    A.typ_s = dr("typ_s", (NTP, P), I32)
    A.ea_s = dr("ea_s", (EP, DE), F32)
    A.rows_d = dr("rows_d", (2, NS), I32)
    A.ix0_d = dr("ix0_d", (P, NTP), I32)
    A.ix1_d = dr("ix1_d", (P, NTP), I32)
    A.typ_d = dr("typ_d", (P, NS), F32)
    A.cont_d = dr("cont_d", (P, NS), F32)
    A.Btab = dr("Btab", (NP, D), F32)
    A.Ztab = dr("Ztab", (NP * R, ZW), F32)
    A.out = nc.dram_tensor("out_x", (N, D), F32, kind="ExternalOutput").ap()
    build(nc, A)
    return run(nc, [feed], core_ids=[0]).results[0]["out_x"]
```
